# Optimizing a Trainium2 kernel written in Bass

```python
import numpy as np
import jax
import jax.numpy as jnp

def _softmax(x, axis=-1):
    return jax.nn.softmax(x, axis=axis)

def _gelu(x):
    return jax.nn.gelu(x, approximate=True)

def _silu(x):
    return jax.nn.silu(x)

def _sigmoid(x):
    return jax.nn.sigmoid(x)

def _layernorm(x, axis=-1, eps=1e-05):
    m = jnp.mean(x, axis=axis, keepdims=True)
    v = jnp.var(x, axis=axis, keepdims=True)
    return (x - m) / jnp.sqrt(v + eps)

def _scatter_add(tgt, idx, src, axis=0):
    return tgt.at[idx].add(src)

def _segment_sum(src, seg, n):
    return jax.ops.segment_sum(src, seg, n)
kernel_name = 'mk_flamingo_gated_d2_seqx_r8_1baa48'

def setup_inputs(seed: int=0):
    np.random.seed(seed)
    _w = jnp.asarray

    def _rec_inputs():
        import jax
        import jax.numpy as jnp
        _rk = jax.random.key(seed)
        x = -0.0003929 + 0.9999 * jax.random.normal(jax.random.fold_in(_rk, 1), (16, 256, 128), jnp.float32)
        _lenS = 256 - jax.random.randint(jax.random.fold_in(_rk, 7), (16,), 0, max(1, 256 // 4) + 1, jnp.int32)
        _lenS2 = 1601 - jax.random.randint(jax.random.fold_in(_rk, 8), (16,), 0, max(1, 1601 // 4) + 1, jnp.int32)
        _ctx_1024P = jax.random.normal(jax.random.fold_in(_rk, 11), (16, 16, 128), jnp.float32)
        _ctx_1024c = jax.random.dirichlet(jax.random.fold_in(_rk, 511), 0.3 * jnp.ones((16,), jnp.float32), (16, 1601))
        _ctx_1024t = jnp.einsum('bsk,bkd->bsd', _ctx_1024c, _ctx_1024P)
        _ctx_1024t = _ctx_1024t * jax.lax.rsqrt(jnp.mean(jnp.square(_ctx_1024t)) + 1e-12) * 0.953939
        ctx_1024 = 2.81802e-05 + 1.00001 * (_ctx_1024t + 0.3 * jax.random.normal(jax.random.fold_in(_rk, 611), (16, 1601, 128), jnp.float32))
        _validS = jnp.arange(256)[None, :] < _lenS[:, None]
        _validS2 = jnp.arange(1601)[None, :] < _lenS2[:, None]
        _causal = jnp.tril(jnp.ones((256, 256), dtype=bool))
        mask_1x1xSxS2_ik0 = jnp.where(jnp.broadcast_to(_validS2[0:1, None, None, :], (1, 1, 256, 1601)), 0, 1).astype(jnp.int32)
        _g = jax.random.normal(jax.random.fold_in(_rk, 9001), (2, 2), jnp.float32)
        _g = jnp.sign(_g) * jnp.maximum(jnp.abs(_g), 1.0) + (_g == 0) * 1.0
        g_xattn = _g[0]
        g_ffn = _g[1]
        return (x, ctx_1024, mask_1x1xSxS2_ik0, g_xattn, g_ffn)
    x, ctx_1024, mask_1x1xSxS2_ik0, g_xattn, g_ffn = _rec_inputs()

    def _L0_xattn_setup():
        import jax, jax.numpy as jnp
        import numpy as np
        QUERY_DIM = 128
        HIDDEN_DIM = 128
        key = jax.random.key(seed)
        k1, k2, k3, k4 = jax.random.split(key, 4)
        query = jax.random.normal(k1, (8, 256, QUERY_DIM), dtype=jnp.float32)
        info = jax.random.normal(k2, (8, 256, HIDDEN_DIM), dtype=jnp.float32)
        bound = 1.0 / np.sqrt(QUERY_DIM)
        W = jax.random.uniform(k3, (HIDDEN_DIM, QUERY_DIM), jnp.float32, -bound, bound)
        b = jax.random.uniform(k4, (HIDDEN_DIM,), jnp.float32, -bound, bound)
        return {'query': query, 'info': info, 'W': W, 'b': b}
    _L0_xattn_all = _L0_xattn_setup()
    _L0_xattn_in = {k: v for k, v in _L0_xattn_all.items() if k in ('W', 'b')}
    del _L0_xattn_all

    def _L0_ffn_setup():
        import jax, jax.numpy as jnp
        import numpy as np
        D_MODEL = 128
        N_EXPERTS = 16
        TOP_K = 2
        EXPERT_DIM = 128
        SHARED_DIM = 256
        B, T = (2, 128)
        key = jax.random.key(seed)
        ks = jax.random.split(key, 7)
        std = 0.02
        return {'x': jax.random.normal(ks[0], (B, T, D_MODEL), dtype=jnp.float32), 'router_w': jax.random.normal(ks[1], (N_EXPERTS, D_MODEL), dtype=jnp.float32) * std, 'gate_up_w': jax.random.normal(ks[2], (N_EXPERTS, D_MODEL, 2 * EXPERT_DIM), dtype=jnp.float32) * std, 'down_w': jax.random.normal(ks[3], (N_EXPERTS, EXPERT_DIM, D_MODEL), dtype=jnp.float32) * std, 'shared_gate_w': jax.random.normal(ks[4], (SHARED_DIM, D_MODEL), dtype=jnp.float32) * std, 'shared_up_w': jax.random.normal(ks[5], (SHARED_DIM, D_MODEL), dtype=jnp.float32) * std, 'shared_down_w': jax.random.normal(ks[6], (D_MODEL, SHARED_DIM), dtype=jnp.float32) * std}
    _L0_ffn_all = _L0_ffn_setup()
    _L0_ffn_in = {k: v for k, v in _L0_ffn_all.items() if k in ('router_w', 'gate_up_w', 'down_w', 'shared_gate_w', 'shared_up_w', 'shared_down_w')}
    del _L0_ffn_all

    def _L1_xattn_setup():
        import jax, jax.numpy as jnp
        import numpy as np
        D_MODEL = 128
        HEADS = 16
        D_K = D_MODEL // HEADS
        B, S = (2, 256)
        key = jax.random.key(seed)
        k1, k2, k3, k4, k5, k6, k7 = jax.random.split(key, 7)
        scale = 1.0 / np.sqrt(D_MODEL)
        inp = {'q_src': jax.random.normal(k1, (B, S, D_MODEL), jnp.float32), 'k_src': jax.random.normal(k2, (B, S, D_MODEL), jnp.float32), 'v_src': jax.random.normal(k3, (B, S, D_MODEL), jnp.float32), 'mask': jnp.tril(jnp.ones((S, S), jnp.int32))[None, None], 'Wq': jax.random.normal(k4, (D_MODEL, D_MODEL), jnp.float32) * scale, 'Wk': jax.random.normal(k5, (D_MODEL, D_MODEL), jnp.float32) * scale, 'Wv': jax.random.normal(k6, (D_MODEL, D_MODEL), jnp.float32) * scale, 'Wo': jax.random.normal(k7, (D_MODEL, D_MODEL), jnp.float32) * scale}
        return inp
    _L1_xattn_all = _L1_xattn_setup()
    _L1_xattn_in = {k: v for k, v in _L1_xattn_all.items() if k in ('Wq', 'Wk', 'Wv', 'Wo')}
    del _L1_xattn_all

    def _L1_ffn_setup():
        import jax, jax.numpy as jnp
        import numpy as np
        BLOCK = 32
        W_BITS = 4
        ACT_BITS = 16

        def act_qdq(x):
            qmax = 2.0 ** (ACT_BITS - 1) - 1.0
            scale = jnp.maximum(jnp.max(jnp.abs(x)) / qmax, 1e-12)
            return jnp.clip(jnp.round(x / scale), -qmax - 1.0, qmax) * scale

        def fixed_qdq_u16(x):
            scale = 1.0 / 65536.0
            return jnp.clip(jnp.round(x / scale), 0.0, 65535.0) * scale

        def lpbq_dequant(w):
            O, I = w.shape
            qmax = 2.0 ** (W_BITS - 1) - 1.0
            wb = w.reshape(O, I // BLOCK, BLOCK)
            s = jnp.maximum(jnp.max(jnp.abs(wb), axis=-1, keepdims=True) / qmax, 1e-12)
            wq = jnp.clip(jnp.round(wb / s), -qmax - 1.0, qmax) * s
            return wq.reshape(O, I)
        key = jax.random.key(seed)
        k1, k2, k3, k4 = jax.random.split(key, 4)
        B, S, H, I = (2, 512, 128, 384)
        x = jax.random.normal(k1, (B, S, H), jnp.float32)
        w_gate = jax.random.normal(k2, (I, H), jnp.float32) * 0.02
        w_up = jax.random.normal(k3, (I, H), jnp.float32) * 0.02
        w_down = jax.random.normal(k4, (H, I), jnp.float32) * 0.02
        return {'x': x, 'w_gate': w_gate, 'w_up': w_up, 'w_down': w_down}
    _L1_ffn_all = _L1_ffn_setup()
    _L1_ffn_in = {k: v for k, v in _L1_ffn_all.items() if k in ('w_gate', 'w_up', 'w_down')}
    del _L1_ffn_all
    return {'x': x, 'ctx_1024': ctx_1024, 'mask_1x1xSxS2_ik0': mask_1x1xSxS2_ik0, 'g_xattn': g_xattn, 'g_ffn': g_ffn, 'L0_xattn_W': _L0_xattn_in['W'], 'L0_xattn_b': _L0_xattn_in['b'], 'L0_ffn_router_w': _L0_ffn_in['router_w'], 'L0_ffn_gate_up_w': _L0_ffn_in['gate_up_w'], 'L0_ffn_down_w': _L0_ffn_in['down_w'], 'L0_ffn_shared_gate_w': _L0_ffn_in['shared_gate_w'], 'L0_ffn_shared_up_w': _L0_ffn_in['shared_up_w'], 'L0_ffn_shared_down_w': _L0_ffn_in['shared_down_w'], 'L1_xattn_Wq': _L1_xattn_in['Wq'], 'L1_xattn_Wk': _L1_xattn_in['Wk'], 'L1_xattn_Wv': _L1_xattn_in['Wv'], 'L1_xattn_Wo': _L1_xattn_in['Wo'], 'L1_ffn_w_gate': _L1_ffn_in['w_gate'], 'L1_ffn_w_up': _L1_ffn_in['w_up'], 'L1_ffn_w_down': _L1_ffn_in['w_down']}

def reference(x, ctx_1024, mask_1x1xSxS2_ik0, g_xattn, g_ffn, L0_xattn_W, L0_xattn_b, L0_ffn_router_w, L0_ffn_gate_up_w, L0_ffn_down_w, L0_ffn_shared_gate_w, L0_ffn_shared_up_w, L0_ffn_shared_down_w, L1_xattn_Wq, L1_xattn_Wk, L1_xattn_Wv, L1_xattn_Wo, L1_ffn_w_gate, L1_ffn_w_up, L1_ffn_w_down):
    import jax
    import jax.numpy as jnp

    def _L0_xattn_ref(query, info, W, b):
        import jax, jax.numpy as jnp
        import numpy as np
        QUERY_DIM = 128
        HIDDEN_DIM = 128
        q = jnp.einsum('bsq,hq->bsh', query, W) + b
        scores = jax.nn.softmax(jnp.einsum('bsh,bmh->bsm', q, info), axis=-1)
        return jnp.einsum('bsm,bmh->bsh', scores, info)

    def _L0_ffn_ref(x, router_w, gate_up_w, down_w, shared_gate_w, shared_up_w, shared_down_w):
        import jax, jax.numpy as jnp
        import numpy as np
        D_MODEL = 128
        N_EXPERTS = 16
        TOP_K = 2
        EXPERT_DIM = 128
        SHARED_DIM = 256
        B, T = (2, 128)
        Bb, Tt, C = x.shape
        N = Bb * Tt
        E = gate_up_w.shape[0]
        logits = jnp.einsum('btc,ec->bte', x, router_w)
        top_vals, top_idx = jax.lax.top_k(logits, TOP_K)
        gates = jax.nn.sigmoid(top_vals)
        xf = x.reshape(N, C)
        sel = top_idx.reshape(N, TOP_K)
        gw = gates.reshape(N, TOP_K)
        w_full = jnp.zeros((N, E), dtype=x.dtype).at[jnp.arange(N)[:, None], sel].add(gw)
        gu = jnp.einsum('nc,ech->neh', xf, gate_up_w)
        gate, up = jnp.split(gu, 2, axis=-1)
        h = jax.nn.silu(gate) * up
        out_all = jnp.einsum('neh,ehc->nec', h, down_w)
        moe = jnp.einsum('ne,nec->nc', w_full, out_all).reshape(Bb, Tt, C)
        sg = jnp.einsum('btc,sc->bts', x, shared_gate_w)
        su = jnp.einsum('btc,sc->bts', x, shared_up_w)
        shared = jnp.einsum('bts,cs->btc', jax.nn.silu(sg) * su, shared_down_w)
        return moe + shared

    def _L1_xattn_ref(q_src, k_src, v_src, mask, Wq, Wk, Wv, Wo):
        import jax, jax.numpy as jnp
        import numpy as np
        D_MODEL = 128
        HEADS = 16
        D_K = D_MODEL // HEADS
        B, S = (2, 256)
        q = q_src @ Wq.T
        k = k_src @ Wk.T
        v = v_src @ Wv.T

        def split_heads(x):
            b, s, _ = x.shape
            return x.reshape(b, s, HEADS, D_K).transpose(0, 2, 1, 3)
        q, k, v = (split_heads(q), split_heads(k), split_heads(v))
        logits = jnp.einsum('bhqd,bhkd->bhqk', q, k) / np.sqrt(D_K)
        logits = jnp.where(mask == 0, jnp.float32(-1000000000.0), logits)
        probs = jax.nn.softmax(logits, axis=-1)
        a = jnp.einsum('bhqk,bhkd->bhqd', probs, v)
        a = a.transpose(0, 2, 1, 3).reshape(q_src.shape[0], -1, D_MODEL)
        return a @ Wo.T

    def _L1_ffn_ref(x, w_gate, w_up, w_down):
        import jax, jax.numpy as jnp
        import numpy as np
        BLOCK = 32
        W_BITS = 4
        ACT_BITS = 16

        def act_qdq(x):
            qmax = 2.0 ** (ACT_BITS - 1) - 1.0
            scale = jnp.maximum(jnp.max(jnp.abs(x)) / qmax, 1e-12)
            return jnp.clip(jnp.round(x / scale), -qmax - 1.0, qmax) * scale

        def fixed_qdq_u16(x):
            scale = 1.0 / 65536.0
            return jnp.clip(jnp.round(x / scale), 0.0, 65535.0) * scale

        def lpbq_dequant(w):
            O, I = w.shape
            qmax = 2.0 ** (W_BITS - 1) - 1.0
            wb = w.reshape(O, I // BLOCK, BLOCK)
            s = jnp.maximum(jnp.max(jnp.abs(wb), axis=-1, keepdims=True) / qmax, 1e-12)
            wq = jnp.clip(jnp.round(wb / s), -qmax - 1.0, qmax) * s
            return wq.reshape(O, I)
        x = act_qdq(x)
        up = act_qdq(x @ lpbq_dequant(w_up).T)
        gate = act_qdq(x @ lpbq_dequant(w_gate).T)
        sig = fixed_qdq_u16(jax.nn.sigmoid(gate))
        gate = act_qdq(gate * sig)
        o = act_qdq(gate * up)
        return o @ lpbq_dequant(w_down).T
    x = x + jnp.tanh(g_xattn[0]) * _L0_xattn_ref(_layernorm(x, axis=-1), ctx_1024, L0_xattn_W, L0_xattn_b)
    x = x + jnp.tanh(g_ffn[0]) * _L0_ffn_ref(_layernorm(x, axis=-1), L0_ffn_router_w, L0_ffn_gate_up_w, L0_ffn_down_w, L0_ffn_shared_gate_w, L0_ffn_shared_up_w, L0_ffn_shared_down_w)
    x = x + jnp.tanh(g_xattn[1]) * _L1_xattn_ref(_layernorm(x, axis=-1), ctx_1024, ctx_1024, mask_1x1xSxS2_ik0, L1_xattn_Wq, L1_xattn_Wk, L1_xattn_Wv, L1_xattn_Wo)
    x = x + jnp.tanh(g_ffn[1]) * _L1_ffn_ref(_layernorm(x, axis=-1), L1_ffn_w_gate, L1_ffn_w_up, L1_ffn_w_down)
    return x

_drawn_inputs = setup_inputs


def setup_inputs(seed=0):
    import zlib

    import numpy as np

    out = dict(_drawn_inputs(seed))
    spreads = {'g_ffn': (-1.0, 0.6)}
    factors = {'L0_ffn_router_w': 8.0,
     'L0_ffn_gate_up_w': 8.0,
     'L0_ffn_down_w': 8.0,
     'L0_ffn_shared_gate_w': 8.0,
     'L0_ffn_shared_up_w': 8.0,
     'L0_ffn_shared_down_w': 8.0,
     'L1_ffn_w_gate': 8.0,
     'L1_ffn_w_up': 8.0,
     'L1_ffn_w_down': 8.0}
    for name, (base, spread) in spreads.items():
        noise = np.random.default_rng([zlib.crc32(name.encode()), seed]).standard_normal(out[name].shape)
        drawn = base * np.exp(spread * noise) if base else spread * noise
        out[name] = jnp.asarray(drawn.astype(out[name].dtype))
    for name, factor in factors.items():
        out[name] = (out[name] * factor).astype(out[name].dtype)
    return out
```

```python
from contextlib import ExitStack

import numpy as np
import concourse.bass as bass
from concourse import mybir

F32 = mybir.dt.float32
BF16 = mybir.dt.bfloat16
I32 = mybir.dt.int32
U32 = mybir.dt.uint32
ALU = mybir.AluOpType
ACT = mybir.ActivationFunctionType
AX = mybir.AxisListType

P = 128
B, S, D = 16, 256, 128
KEYS = 1601
TT = S // P
KT = -(-KEYS // P)
KLAST = KEYS - (KT - 1) * P
BANK = 512
EPS = 1e-5
NEXP, NSH = 16, 2
NE = NEXP + NSH
HEADS, DK = 16, 8
GRP = 4
VW = 32
MASKED = -float(2 ** 100)
FF = 384
FC = FF // P
BLK = 32
QMAX = 32767.0
RND = 1.5 * 2.0 ** 23


def wait(eng, sem, value, turns=None):
    if isinstance(value, int) and value <= 0:
        return
    eng.wait_ge(sem, value)
    if turns is not None:
        eng.sem_inc(turns, 1)


def wait_alone(eng, sem, value, turns):
    eng.wait_ge(sem, value)
    eng.sem_inc(turns, 1)


class Chain:

    def __init__(self, eng, sem, per_round, r):
        self.eng, self.sem, self.per, self.base, self.n = eng, sem, per_round, per_round * r, 0

    def mark(self, ins):
        ins.then_inc(self.sem, 1)
        self.n += 1

    def sync(self, turns=None):
        self.eng.wait_ge(self.sem, self.base + self.n)
        if turns is not None:
            self.eng.sem_inc(turns, 1)

    def end(self):
        assert self.n == self.per, (self.n, self.per)


def key_rows(t):
    return P if t < KT - 1 else KLAST


class Mem:

    def __init__(self, nc, ctx, g=None):
        self.nc, self.ctx, self.g = nc, ctx, g

    def sb(self, name, shape, dt=F32):
        return self.ctx.enter_context(self.nc.sbuf_tensor(name, shape, dt))

    def ps(self, name, cols, dt=F32):
        return self.ctx.enter_context(self.nc.psum_tensor(name, [P, cols], dt))

    def sem(self, name):
        if name not in self.g["sems"]:
            self.g["sems"][name] = self.g["ctx"].enter_context(self.nc.semaphore(name))
        return self.g["sems"][name]

    def sems(self, names):
        return {n: self.sem(n) for n in names.split()}


def build_setup(nc, d, g):
    with ExitStack() as ctx:
        m = Mem(nc, ctx, g)
        mask_q = m.sb("mask_q", [P, TT, KEYS], I32)
        seen = m.sb("seen", [P, TT, KEYS])
        ones = m.sb("ones_col", [P, 1])
        row = m.sb("count_row", [1, KEYS])
        row2 = m.sb("count_row2", [1, KEYS])
        st = m.sb("mask_stats", [1, 8])
        anyr = m.sb("anyr", [P, TT])
        gates = m.sb("gates", [P, 4])
        cnt = m.ps("cnt", 4 * BANK)
        s = m.sems("id_zero id_done iota_done mask_in gate_in vec cnt_done tanh_done")
        block = ctx.enter_context(nc.Block())

        @block.sync
        def _(sp):
            sp.dma_start(mask_q[:], d["mask"].rearrange("a b (t p) k -> p (a b t) k", p=P)).then_inc(s["mask_in"], 16)
            sp.dma_start(gates[:, 0:2], d["g_xattn"].rearrange("(a n) -> a n", a=1).broadcast_to([P, 2])).then_inc(s["gate_in"], 16)
            sp.dma_start(gates[:, 2:4], d["g_ffn"].rearrange("(a n) -> a n", a=1).broadcast_to([P, 2])).then_inc(s["gate_in"], 16)

        @block.gpsimd
        def _(pool):
            nc.gpsimd.memset(g["ident"][:], 0.0).then_inc(s["id_zero"], 1)
            nc.gpsimd.memset(g["identb"][:], 0.0).then_inc(s["id_zero"], 1)
            pool.wait_ge(s["id_zero"], 2)
            for t in (g["ident"], g["identb"]):
                nc.gpsimd.affine_select(out=t[:], in_=t[:], compare_op=ALU.not_equal, fill=1.0, base=0,
                                        pattern=[[-1, P]], channel_multiplier=1).then_inc(s["id_done"], 1)
            nc.gpsimd.iota(g["iota_i"][:], pattern=[[1, NEXP]], base=0, channel_multiplier=0).then_inc(s["iota_done"], 1)
            nc.gpsimd.memset(g["mhalf"][:], -0.5).then_inc(s["iota_done"], 1)
            nc.gpsimd.memset(g["eps"][:], EPS).then_inc(s["iota_done"], 1)

        @block.scalar
        def _(act):
            act.wait_ge(s["gate_in"], 32)
            nc.scalar.activation(g["tgate"][:], gates[:], ACT.Tanh).then_inc(s["tanh_done"], 1)

        @block.vector
        def _(dve):
            v = Chain(dve, s["vec"], 0, 0)
            v.mark(nc.vector.memset(ones[:], 1.0))
            dve.wait_ge(s["iota_done"], 1)
            v.mark(nc.vector.tensor_copy(g["iota"][:], g["iota_i"][:]))
            dve.wait_ge(s["mask_in"], 16)
            v.mark(nc.vector.tensor_scalar(seen[:], mask_q[:], 0.0, None, ALU.not_equal))
            v.sync()
            v.mark(nc.vector.tensor_reduce(anyr[:], seen[:], AX.X, ALU.max))
            v.sync()
            v.mark(nc.vector.tensor_copy(g["any_q"][:], anyr[:]))
            dve.wait_ge(s["cnt_done"], 1)
            v.mark(nc.vector.tensor_copy(row[:], cnt[0:1, 0:KEYS]))
            v.sync()
            v.mark(nc.vector.tensor_scalar(row2[:], row[:], -1.0, float(S), ALU.mult, ALU.add))
            v.sync()
            v.mark(nc.vector.tensor_tensor(row2[:], row2[:], row[:], ALU.mult))
            v.sync()
            v.mark(nc.vector.tensor_reduce(st[:, 0:1], row2[:], AX.X, ALU.add))
            v.mark(nc.vector.tensor_reduce(st[:, 1:2], row[:, 0:KEYS - BANK], AX.X, ALU.add))
            v.mark(nc.vector.tensor_reduce(st[:, 2:3], row[:], AX.X, ALU.add))
            v.mark(nc.vector.tensor_scalar(g["bias_row"][:], row[:, KEYS - BANK:KEYS], 0.0, MASKED, ALU.is_equal, ALU.mult))
            v.sync()
            v.mark(nc.vector.tensor_tensor(st[:, 3:4], st[:, 0:1], st[:, 1:2], ALU.add))
            v.sync()
            v.mark(nc.vector.tensor_scalar(st[:, 4:5], st[:, 3:4], 0.0, None, ALU.is_equal))
            v.mark(nc.vector.tensor_scalar(st[:, 5:6], st[:, 2:3], 0.0, None, ALU.is_gt))
            v.sync()
            v.mark(nc.vector.tensor_tensor(g["tail_only"][:], st[:, 4:5], st[:, 5:6], ALU.mult))
            v.sync()

        @block.tensor
        def _(pe):
            pe.wait_ge(s["vec"], 3)
            for c in range(4):
                w = min(BANK, KEYS - c * BANK)
                for t in range(TT):
                    last = nc.tensor.matmul(cnt[0:1, c * BANK:c * BANK + w], ones[:], seen[:, t, c * BANK:c * BANK + w],
                                            start=(t == 0), stop=(t == TT - 1))
            last.then_inc(s["cnt_done"], 1)


def build_attend_moe(nc, d, g):
    with ExitStack() as ctx:
        m = Mem(nc, ctx, g)
        ident, tgate = g["ident"], g["tgate"]
        wT = m.sb("wT", [P, P])
        wb = m.sb("wb", [P, 1])
        rwT = m.sb("rwT", [P, NEXP])
        gu_w = m.sb("gu_w", [P, NE, 2 * P])
        dn_w = m.sb("dn_w", [P, NE, P])
        ctxn = [m.sb(f"ctxn{j}", [P, KT, P]) for j in range(2)]
        ctxT = [m.sb(f"ctxT{j}", [P, KEYS]) for j in range(2)]
        x0 = [m.sb(f"x0_{j}", [P, TT, D]) for j in range(2)]
        x1 = [m.sb(f"x1_{j}", [P, TT, D]) for j in range(2)]
        a_st, a_mv, a_ve, a_rs = (m.sb("a_" + n, sh) for n, sh in
                                  (("st", [P, TT, 6]), ("mv", [P, TT, 2]), ("ve", [P, TT]), ("rs", [P, TT])))
        a_xn, a_xnT, a_qT = m.sb("a_xn", [P, TT, D]), m.sb("a_xnT", [P, S]), m.sb("a_qT", [P, S])
        probs = m.sb("probs", [P, KEYS])
        probsT = m.sb("probsT", [P, KT, P])
        a_nm, a_sum, a_rec, a_f = (m.sb("a_" + n, [P, TT]) for n in ("nm", "sum", "rec", "f"))
        b_st, b_mv, b_ve, b_rs = (m.sb("b_" + n, sh) for n, sh in
                                  (("st", [P, TT, 6]), ("mv", [P, TT, 2]), ("ve", [P, TT]), ("rs", [P, TT])))
        b_xn, b_xnT = m.sb("b_xn", [P, TT, D]), m.sb("b_xnT", [P, S])
        lg = m.sb("lg", [P, TT, NEXP])
        top = m.sb("top", [P, TT, 8])
        topi = m.sb("topi", [P, TT, 8], U32)
        topf = m.sb("topf", [P, TT, 8])
        tth = m.sb("tth", [P, TT, 2])
        gt2 = m.sb("gt2", [P, TT, 2])
        oh = m.sb("oh", [P, TT, 2, NEXP])
        ew = m.sb("ew", [P, TT, NE])
        th = [m.sb(f"th{j}", [P, S]) for j in range(2)]
        ha = [m.sb(f"ha{j}", [P, S]) for j in range(2)]
        h = [m.sb(f"h{j}", [P, S]) for j in range(2)]
        acc = m.sb("acc", [P, TT, D])
        sc = m.ps("sc", 4 * BANK)
        misc = m.ps("misc", BANK)
        gu = [m.ps(f"gu{j}", BANK) for j in range(2)]
        eo = m.ps("eo", BANK)

        s = m.sems("w_in a_mv a_rstd a_xn a_xnT_ps a_xnT a_q_ps a_q a_s a_max a_exp a_tr a_evv a_evs a_o a_x1 a_ch a_pc "
                   "b_mv b_rstd b_xn b_xnT_ps b_xnT b_lg_ps b_lg b_top b_tth b_w b_gu b_th b_ha b_h b_out b_acc b_x2 b_ch b_pc turns turns_s")
        s["w2_in"] = m.sem("w2_in")
        x_in = [m.sem(f"x_in{j}") for j in range(2)]
        ctxT_in = [m.sem(f"ctxT_in{j}") for j in range(2)]
        ctxn_in = [m.sem(f"ctxn_in{j}") for j in range(2)]
        block = ctx.enter_context(nc.Block())
        EV_V = [(0, 4), (8, 12)]
        EV_S = [(4, 8), (12, 13)]

        def steps(eng, run):
            run((0, 0, 0), None)
            run((1, 1, 0), (0, 0, 0))
            with eng.Fori(1, B // 2) as i:
                run((i * 2, 0, i), (i * 2 - 1, 1, i - 1))
                run((i * 2 + 1, 1, i), (i * 2, 0, i))
            run(None, (B - 1, 1, B // 2 - 1))

        @block.sync
        def _(sp):
            sp.dma_start(wT[:], d["L0_WT"]).then_inc(s["w_in"], 16)
            sp.dma_start(wb[:], d["L0_xattn_b"].rearrange("(p a) -> p a", a=1)).then_inc(s["w_in"], 16)
            sp.dma_start(rwT[:], d["router_wT"]).then_inc(s["w_in"], 16)

            def load(b, j):
                wait(sp, s["a_x1"], TT * (b - 1), s["turns_s"])
                sp.dma_start(x0[j][:], d["x"][b].rearrange("(t p) c -> p t c", p=P)).then_inc(x_in[j], 16)
                sp.dma_start(ctxT[j][:], d["ctxT"][b]).then_inc(ctxT_in[j], 16)
                full = (KT - 1) * P
                sp.dma_start(ctxn[j][:, 0:KT - 1, :], d["ctx"][b, 0:full].rearrange("(t p) c -> p t c", p=P)).then_inc(ctxn_in[j], 16)
                sp.dma_start(ctxn[j][0:KLAST, KT - 1, :], d["ctx"][b, full:KEYS]).then_inc(ctxn_in[j], 16)

            load(0, 0)
            load(1, 1)
            gu = d["gate_up_w"].rearrange("e c n -> c e n")
            sp.dma_start(gu_w[:, 0:NEXP, :], gu).then_inc(s["w2_in"], 16)
            for n, w in enumerate((d["shared_gateT"], d["shared_upT"])):
                sp.dma_start(gu_w[:, NEXP:NE, n * P:(n + 1) * P], w.rearrange("c (e n) -> c e n", e=NSH)).then_inc(s["w2_in"], 16)
            sp.dma_start(dn_w[:, 0:NEXP, :], d["down_w"].rearrange("e h c -> h e c")).then_inc(s["w2_in"], 16)
            sp.dma_start(dn_w[:, NEXP:NE, :], d["shared_downT"].rearrange("(e h) c -> h e c", e=NSH)).then_inc(s["w2_in"], 16)
            with sp.Fori(1, B // 2) as i:
                load(i * 2, 0)
                load(i * 2 + 1, 1)

        @block.gpsimd
        def _(pool):
            def rstd(b, mv, ve, rs, mv_sem, out_sem, ch):
                pool.wait_ge(mv_sem, b + 1)
                nc.gpsimd.tensor_tensor(ve[:], mv[:, :, 1], g["eps"][:], ALU.add).then_inc(ch, 1)
                pool.wait_ge(ch, b + 1)
                nc.gpsimd.tensor_tensor(rs[:], ve[:], g["mhalf"][:], ALU.pow).then_inc(out_sem, 1)

            def run(a, b):
                if b is not None:
                    rstd(b[0], b_mv, b_ve, b_rs, s["b_mv"], s["b_rstd"], s["b_pc"])
                if a is not None:
                    rstd(a[0], a_mv, a_ve, a_rs, s["a_mv"], s["a_rstd"], s["a_pc"])
            steps(pool, run)

        @block.tensor
        def _(pe):
            pe.wait_ge(s["w_in"], 48)

            def run(a, b):
                if b is not None:
                    n, j, r = b
                    pe.wait_ge(s["b_xn"], n + 1)
                    for t in range(TT):
                        last = nc.tensor.transpose(misc[:, S + t * P:S + t * P + P], b_xn[:, t, :], ident[:])
                    last.then_inc(s["b_xnT_ps"], 1)
                if a is not None:
                    n, j, r = a
                    pe.wait_ge(s["a_xn"], n + 1)
                    wait(pe, s["a_x1"], TT * n)
                    for t in range(TT):
                        last = nc.tensor.transpose(misc[:, t * P:t * P + P], a_xn[:, t, :], ident[:])
                    last.then_inc(s["a_xnT_ps"], 1)
                if b is not None:
                    pe.wait_ge(s["b_xnT"], b[0] + 1)
                if a is not None:
                    pe.wait_ge(s["a_xnT"], a[0] + 1)
                    nc.tensor.matmul(misc[:, 0:S], wT[:], a_xnT[:], start=True, stop=True).then_inc(s["a_q_ps"], 1)
                if b is not None:
                    for t in range(TT):
                        last = nc.tensor.matmul(misc[:, S + t * NEXP:S + (t + 1) * NEXP], b_xnT[:, t * P:(t + 1) * P], rwT[:],
                                                start=True, stop=True)
                    last.then_inc(s["b_lg_ps"], 1)

                def qk(t):
                    n, j, r = a
                    if t == 0:
                        pe.wait_ge(s["a_q"], n + 1)
                        pe.wait_ge(ctxT_in[j], (r + 1) * 16)
                    wait(pe, s["a_evv"], TT * n + t)
                    wait(pe, s["a_evs"], TT * n + t)
                    for c in range(4):
                        w = min(BANK, KEYS - c * BANK)
                        last = nc.tensor.matmul(sc[:, c * BANK:c * BANK + w], a_qT[:, t * P:(t + 1) * P],
                                                ctxT[j][:, c * BANK:c * BANK + w], start=True, stop=True)
                    last.then_inc(s["a_s"], 1)

                def tr(t):
                    n, j, r = a
                    pe.wait_ge(s["a_exp"], TT * n + t + 1)
                    for k in range(KT):
                        w = key_rows(k)
                        last = nc.tensor.transpose(sc[0:w, k * P:(k + 1) * P], probs[:, k * P:k * P + w], ident[:])
                    last.then_inc(s["a_tr"], 1)

                def pv(t):
                    n, j, r = a
                    if t == 0:
                        pe.wait_ge(ctxn_in[j], (r + 1) * 32)
                        if b is not None:
                            pe.wait_ge(s["b_lg"], b[0] + 1)
                    else:
                        pe.wait_ge(s["a_x1"], TT * n + t)
                    pe.wait_ge(s["a_evv"], TT * n + t + 1)
                    pe.wait_ge(s["a_evs"], TT * n + t + 1)
                    for k in range(KT):
                        w = key_rows(k)
                        last = nc.tensor.matmul(misc[:, 0:D], probsT[0:w, k, :], ctxn[j][0:w, k, :],
                                                start=(k == 0), stop=(k == KT - 1))
                    last.then_inc(s["a_o"], 1)

                def expert_up(e):
                    n, j, r = b
                    wait(pe, s["b_h"], NE * n + e - 1)
                    nc.tensor.matmul(gu[e % 2][:, 0:S], gu_w[:, e, 0:P], b_xnT[:], start=True, stop=True)
                    nc.tensor.matmul(gu[e % 2][:, S:2 * S], gu_w[:, e, P:2 * P], b_xnT[:], start=True, stop=True).then_inc(s["b_gu"], 1)

                def expert_down(e):
                    n, j, r = b
                    pe.wait_ge(s["b_h"], NE * n + e + 1)
                    wait(pe, s["b_acc"], NE * n + e)
                    for t in range(TT):
                        last = nc.tensor.matmul(eo[:, t * D:(t + 1) * D], h[e % 2][:, t * P:(t + 1) * P], dn_w[:, e, :],
                                                start=True, stop=True)
                    last.then_inc(s["b_out"], 1)

                att = {0: (qk, 0), 5: (tr, 0), 7: (qk, 1), 9: (pv, 0), 12: (tr, 1), 15: (pv, 1)}
                if b is not None and isinstance(b[0], int) and b[0] == 0:
                    pe.wait_ge(s["w2_in"], 80)
                for e in range(NE):
                    if b is not None:
                        expert_up(e)
                        if e > 0:
                            expert_down(e - 1)
                    if a is not None and e in att:
                        att[e][0](att[e][1])
                if b is not None:
                    expert_down(NE - 1)
            steps(pe, run)

        @block.scalar
        def _(act):
            act.wait_ge(s["w_in"], 48)

            def run(a, b):
                if b is not None:
                    act.wait_ge(s["b_xnT_ps"], b[0] + 1)
                    if a is not None:
                        act.wait_ge(s["a_xnT_ps"], a[0] + 1)
                    wait(act, s["b_gu"], NE * b[0])
                    nc.scalar.activation(b_xnT[:], misc[:, S:2 * S], ACT.Copy).then_inc(s["b_xnT"], 1)
                if a is not None:
                    act.wait_ge(s["a_xnT_ps"], a[0] + 1)
                    nc.scalar.activation(a_xnT[:], misc[:, 0:S], ACT.Copy).then_inc(s["a_xnT"], 1)
                    act.wait_ge(s["a_q_ps"], a[0] + 1)
                    if b is not None:
                        act.wait_ge(s["b_lg_ps"], b[0] + 1)
                        act.wait_ge(s["b_lg"], b[0] + 1)
                    nc.scalar.activation(a_qT[:], misc[:, 0:S], ACT.Identity, bias=wb[:, 0:1]).then_inc(s["a_q"], 1)
                if b is not None:
                    act.wait_ge(s["b_top"], b[0] + 1)
                    nc.scalar.activation(tth[:], top[:, :, 0:2], ACT.Tanh, scale=0.5).then_inc(s["b_tth"], 1)

                def exp(t):
                    n, j, r = a
                    act.wait_ge(s["a_max"], TT * n + t + 1)
                    nc.scalar.activation(probs[:], sc[:, 0:KEYS], ACT.Exp, bias=a_nm[:, t:t + 1],
                                         accum_out=a_sum[:, t:t + 1]).then_inc(s["a_exp"], 1)

                def evac(t):
                    n, j, r = a
                    act.wait_ge(s["a_tr"], TT * n + t + 1)
                    wait(act, s["a_o"], TT * n + t)
                    for k0, k1 in EV_S:
                        w = key_rows(k0) if k1 - k0 == 1 else P
                        last = nc.scalar.activation(probsT[0:w, k0:k1, :].rearrange("p a b -> p (a b)"), sc[0:w, k0 * P:k1 * P], ACT.Copy)
                    last.then_inc(s["a_evs"], 1)

                def tanh(e):
                    n, j, r = b
                    act.wait_ge(s["b_gu"], NE * n + e + 1)
                    nc.scalar.activation(th[e % 2][:], gu[e % 2][:, 0:S], ACT.Tanh, scale=0.5).then_inc(s["b_th"], 1)

                att = {3: (exp, 0), 6: (evac, 0), 10: (exp, 1), 13: (evac, 1)}
                for e in range(NE):
                    if b is not None:
                        tanh(e)
                    if a is not None and e in att:
                        att[e][0](att[e][1])
            steps(act, run)

        @block.vector
        def _(dve):
            nc.vector.memset(ew[:, :, NEXP:NE], 0.5).then_inc(s["b_w"], 1)

            def moments(x, stats, mv, ch, out):
                for t in range(TT):
                    ch.mark(nc.vector.bn_stats(stats[:, t, :], x[:, t, :]))
                ch.sync(s["turns"])
                for t in range(TT):
                    last = nc.vector.bn_aggr(mv[:, t, :], stats[:, t, :])
                    if t == TT - 1:
                        last.then_inc(out, 1)

            def norm(x, xn, mv, rs, out):
                for t in range(TT):
                    last = nc.vector.tensor_scalar(xn[:, t, :], x[:, t, :], mv[:, t, 0:1], rs[:, t:t + 1], ALU.subtract, ALU.mult)
                last.then_inc(out, 1)

            def run(a, b):
                if a is not None:
                    ca = Chain(dve, s["a_ch"], 6, a[0])
                if b is not None:
                    cb = Chain(dve, s["b_ch"], 11, b[0])
                    moments(x1[b[1]], b_st, b_mv, cb, s["b_mv"])
                if a is not None:
                    dve.wait_ge(x_in[a[1]], (a[2] + 1) * 16)
                    moments(x0[a[1]], a_st, a_mv, ca, s["a_mv"])
                if b is not None:
                    dve.wait_ge(s["b_rstd"], b[0] + 1)
                    norm(x1[b[1]], b_xn, b_mv, b_rs, s["b_xn"])
                if a is not None:
                    dve.wait_ge(s["a_rstd"], a[0] + 1)
                    norm(x0[a[1]], a_xn, a_mv, a_rs, s["a_xn"])
                if b is not None:
                    dve.wait_ge(s["b_lg_ps"], b[0] + 1)
                    nc.vector.tensor_copy(lg[:].rearrange("p t e -> p (t e)"), misc[:, S:S + TT * NEXP]).then_inc(s["b_lg"], 1)
                    wait_alone(dve, s["b_lg"], b[0] + 1, s["turns"])
                    for t in range(TT):
                        last = nc.vector.max(top[:, t, :], lg[:, t, :])
                    last.then_inc(s["b_top"], 1)
                    wait_alone(dve, s["b_top"], b[0] + 1, s["turns"])
                    for t in range(TT):
                        cb.mark(nc.vector.max_index(topi[:, t, :], top[:, t, :], lg[:, t, :]))
                    cb.sync()
                    cb.mark(nc.vector.tensor_copy(topf[:], topi[:]))
                    dve.wait_ge(s["b_tth"], b[0] + 1)
                    cb.mark(nc.vector.tensor_scalar(gt2[:], tth[:], 1.0, 0.25, ALU.add, ALU.mult))
                    cb.sync()
                    for t in range(TT):
                        for c in range(2):
                            cb.mark(nc.vector.tensor_scalar(oh[:, t, c, :], g["iota"][:], topf[:, t, c:c + 1], gt2[:, t, c:c + 1],
                                                            ALU.is_equal, ALU.mult))
                    cb.sync()
                    cb.mark(nc.vector.tensor_tensor(ew[:, :, 0:NEXP], oh[:, :, 0, :], oh[:, :, 1, :], ALU.add))

                def negmax(t):
                    n, j, r = a
                    dve.wait_ge(s["a_s"], TT * n + t + 1)
                    nc.vector.tensor_reduce(a_nm[:, t:t + 1], sc[:, 0:KEYS], AX.X, ALU.max, negate=True).then_inc(s["a_max"], 1)

                def evac(t):
                    n, j, r = a
                    dve.wait_ge(s["a_tr"], TT * n + t + 1)
                    wait(dve, s["a_o"], TT * n + t)
                    for k0, k1 in EV_V:
                        last = nc.vector.tensor_copy(probsT[:, k0:k1, :].rearrange("p a b -> p (a b)"), sc[:, k0 * P:k1 * P])
                    last.then_inc(s["a_evv"], 1)

                def update(t):
                    n, j, r = a
                    ca.mark(nc.vector.reciprocal(a_rec[:, t:t + 1], a_sum[:, t:t + 1]))
                    dve.wait_ge(s["a_o"], TT * n + t + 1)
                    ca.sync()
                    ins = nc.vector.tensor_scalar(a_f[:, t:t + 1], a_rec[:, t:t + 1], tgate[:, 0:1], None, ALU.mult)
                    ca.mark(ins)
                    ca.sync()
                    nc.vector.scalar_tensor_tensor(out=x1[j][:, t, :], in0=misc[:, 0:D], scalar=a_f[:, t:t + 1], in1=x0[j][:, t, :],
                                                   op0=ALU.mult, op1=ALU.add).then_inc(s["a_x1"], 1)

                def hidden(e):
                    n, j, r = b
                    dve.wait_ge(s["b_th"], NE * n + e + 1)
                    wait(dve, s["b_h"], NE * n + e - 1)
                    nc.vector.scalar_tensor_tensor(out=ha[e % 2][:], in0=th[e % 2][:], scalar=1.0, in1=gu[e % 2][:, 0:S],
                                                   op0=ALU.add, op1=ALU.mult).then_inc(s["b_ha"], 1)

                def hidden2(e):
                    n, j, r = b
                    dve.wait_ge(s["b_ha"], NE * n + e + 1)
                    wait(dve, s["b_out"], NE * n + e - 1)
                    nc.vector.tensor_tensor(h[e % 2][:], ha[e % 2][:], gu[e % 2][:, S:2 * S], ALU.mult).then_inc(s["b_h"], 1)

                def add(e):
                    n, j, r = b
                    dve.wait_ge(s["b_out"], NE * n + e + 1)
                    if e > 0:
                        dve.wait_ge(s["b_acc"], NE * n + e)
                    else:
                        cb.sync()
                        wait(dve, s["b_x2"], n)
                    for t in range(TT):
                        o = eo[:, t * D:(t + 1) * D]
                        if e == 0:
                            last = nc.vector.tensor_scalar(acc[:, t, :], o, ew[:, t, e:e + 1], None, ALU.mult)
                        else:
                            last = nc.vector.scalar_tensor_tensor(out=acc[:, t, :], in0=o, scalar=ew[:, t, e:e + 1], in1=acc[:, t, :],
                                                                  op0=ALU.mult, op1=ALU.add)
                    last.then_inc(s["b_acc"], 1)

                att = {1: (negmax, 0), 6: (evac, 0), 8: (negmax, 1), 10: (update, 0), 13: (evac, 1), 16: (update, 1)}
                for e in range(NE):
                    if b is not None:
                        hidden(e)
                        if e > 0:
                            add(e - 1)
                        hidden2(e)
                    if a is not None and e in att:
                        att[e][0](att[e][1])
                if b is not None:
                    n, j, r = b
                    add(NE - 1)
                    dve.wait_ge(s["b_acc"], NE * n + NE)
                    nc.vector.scalar_tensor_tensor(out=g["xs"][:, n, :, :].rearrange("p t c -> p (t c)"), in0=acc[:].rearrange("p t c -> p (t c)"),
                                                   scalar=tgate[:, 2:3], in1=x1[j][:].rearrange("p t c -> p (t c)"),
                                                   op0=ALU.mult, op1=ALU.add).then_inc(s["b_x2"], 1)
                if a is not None:
                    n, j, r = a
                    dve.wait_ge(s["a_x1"], TT * n + TT)
            dve.wait_ge(s["b_w"], 1)
            steps(dve, run)
            dve.wait_ge(s["b_x2"], B)


def build_head_attention(nc, d, g, general):
    K0 = 0 if general else KEYS - BANK
    NK = KEYS - K0
    CH = [(c, min(BANK, NK - c)) for c in range(0, NK, BANK)]
    NC = len(CH)
    NT = -(-NK // P)
    NB = 1 if general else 3
    rows = lambda t: min(P, NK - t * P)
    PARTS = [(0, 0), (0, 1), (0, 2), (1, 0), (1, 1), (2, 0)]
    R_BIAS = len(PARTS) * DK
    R_MAX = 96
    R_ALL = R_MAX + 2
    HH = HEADS // 2
    tag = "g" if general else "f"
    with ExitStack() as ctx:
        m = Mem(nc, ctx, g)
        sb = lambda n, sh, dt=F32: m.sb(f"{tag}_{n}", sh, dt)
        ident, tgate, xs = g["ident"], g["tgate"], g["xs"]
        WqT, WkT, WvT, WoT = (sb(n, [P, P]) for n in ("WqT", "WkT", "WvT", "WoT"))
        ct = [sb(f"ct{j}", [P, NK]) for j in range(NB)]
        st6, mv, ve, rs0, rs = sb("st6", [P, TT, 6]), sb("mv", [P, TT, 2]), sb("ve", [P, TT]), sb("rs0", [P, TT]), sb("rs", [P, TT])
        xn, xnT = sb("xn", [P, TT, D]), sb("xnT", [P, S])
        qk = sb("qk", [P, S + NK])
        rem = sb("rem", [P, S + NK])
        parts = sb("parts", [P, 3, S + NK], BF16)
        Q = [sb(f"Q{j}", [R_ALL, HEADS, S], BF16) for j in range(NB)]
        K = [sb(f"K{j}", [R_ALL, HEADS, NK], BF16) for j in range(NB)]
        V = [sb(f"V{j}", [P, NT, HEADS, VW]) for j in range(NB)]
        mx = sb("mx", [P, TT, HEADS])
        mxc = sb("mxc", [P, TT, HEADS, NC])
        nmf = [sb(f"nmf{i}", [HH, S]) for i in range(2)]
        nmp = [sb(f"nmp{i}", [HH, 2, S], BF16) for i in range(2)]
        pr = [sb(f"pr{i}", [P, GRP, 4 * S]) for i in range(2)]
        ots = sb("ots", [P, S])
        rec = sb("rec", [P, TT, GRP])
        att = sb("att", [P, TT, D])
        attT = sb("attT", [P, S])
        if general:
            bias_q = sb("bias_q", [P, TT, KEYS], BF16)
            bias_k = sb("bias_k", [P, NT, S], BF16)
            mask_i = sb("mask_i", [P, KEYS], I32)
            zrow = sb("zrow", [1, KEYS], BF16)
        orow = sb("orow", [1, S], BF16)
        ps = lambda n, c: m.ps(f"{tag}_{n}", c)
        sbank = [ps(f"s{i}", BANK) for i in range(2)]
        stb = [ps(f"st{i}", 2 * BANK) for i in range(2)]
        otb = ps("ot", BANK)
        misc = ps("misc", BANK)
        s = {n: m.sem(f"h_{n}") for n in
             ("w_in init init_v mask_in bias_done rows_in p_mv p_ve p_pow p_rstd p_xn p_ch p_kps p_vps p_kc p_vc p_rem p_mid p_parts "
              "turns turns_p turns_s s_ps s_red s_mx s_mh s_ml t_st t_exp t_pv t_ot t_rec misc_full misc_free").split()}
        mx_done = s["s_mx"] if NC > 1 else s["s_red"]
        ct_in = [m.sem(f"h_ct_in{j}") for j in range(NB)]
        qk_in = [m.sem(f"h_qk_in{j}") for j in range(NB)]
        mx_in = [[m.sem(f"h_mx_in{j}_{i}") for i in range(2)] for j in range(NB)]
        block = ctx.enter_context(nc.Block())

        def at(n, k=0):
            base, rest = n
            r, j = divmod(rest + k, NB)
            return base * NB + rest + k, j, base + r

        def steps(eng, run):
            if general:
                run(at((0, 0)), at((0, 0)), at((0, 0)), at((0, 0)), 0)
                with eng.Fori(1, B) as i:
                    run(at((i, 0)), at((i, 0)), at((i, 0)), at((i, 0)), i * 10)
                return
            run(at((0, 0)), None, None, None, 0)
            run(at((0, 1)), at((0, 0)), None, None, 2)
            run(at((0, 2)), at((0, 1)), at((0, 0)), None, 6)
            run(at((0, 3)), at((0, 2)), at((0, 1)), at((0, 0)), 13)
            with eng.Fori(0, 4) as i:
                for k in range(3):
                    n = (i, 2 + k)
                    run(at(n, 2), at(n, 1), at(n), at(n, -1), i * 30 + (13 + 10 * (1 + k)))
            run(None, at((0, 15)), at((0, 14)), at((0, 13)), 143)
            run(None, None, at((0, 15)), at((0, 14)), 151)
            run(None, None, None, at((0, 15)), 157)

        MISC = {("P", "ln"), ("P", "q"), ("S", "row"), ("T", "turn"), ("E", "turn"), ("E", "attT"), ("E", "wo")}

        def plan(p, s_, t, e, uses):
            for item in order(p, s_, t, e):
                yield (*item, uses)
                if item[:2] in MISC:
                    uses = uses + 1

        def order(p, s_, t, e):
            out = []
            nS = HEADS * TT
            if general:
                out += [("P", "ln", 0), ("P", "q", 0), ("P", "kv", 0), ("P", "split", 0)]
                for u in range(nS):
                    out.append(("S", "max", u))
                    if u in (nS // 2 - 1, nS - 1):
                        out.append(("S", "row", u // (nS // 2)))
                for gi in range(4):
                    for c in range(NC):
                        for hh in range(GRP):
                            out.append(("T", "head", (gi, c, hh)))
                        out.append(("T", "pv", (gi, c)))
                    out.append(("T", "out", gi))
                    if gi < 3:
                        out.append(("T", "turn", gi))
                out += [("E", "turn", 3), ("E", "attT", 0), ("E", "wo", 0)]
                return out
            at_slot = {0: [("P", "ln", 0), ("E", "pv", (3, 0)), ("E", "out", 3)],
                       1: [("P", "q", 0), ("E", "turn", 3)],
                       2: [("P", "kv", 0), ("E", "attT", 0)],
                       3: [("P", "split", 0), ("E", "wo", 0)],
                       4: [("T", "pv", (0, 0)), ("T", "out", 0)], 5: [("T", "turn", 0)],
                       8: [("T", "pv", (1, 0)), ("T", "out", 1)], 9: [("T", "turn", 1), ("S", "row", 0)],
                       12: [("T", "pv", (2, 0)), ("T", "out", 2)], 13: [("T", "turn", 2)],
                       15: [("S", "row", 1)]}
            done = 0
            for h in range(HEADS):
                out.append(("T", "head", (h // GRP, 0, h % GRP)))
                want = max(0, (h - 2) * nS // 13) if h < 15 else nS
                out += [("S", "max", u) for u in range(done, min(want, nS))]
                done = max(done, min(want, nS))
                out += at_slot.get(h, [])
            have = {"P": p, "S": s_, "T": t, "E": e}
            return [x for x in out if have[x[0]] is not None]

        def sent(eng, sems, batch, per):
            n, j, r = batch
            jp, rp = (j - 1, r) if j else (NB - 1, r - 1)
            if not (isinstance(n, int) and n == 0):
                eng.wait_ge(sems[jp], per * (rp + 1))

        @block.sync
        def _(sp):
            for t, n in ((WqT, "WqT"), (WkT, "WkT"), (WvT, "WvT"), (WoT, "WoT")):
                sp.dma_start(t[:], d[n]).then_inc(s["w_in"], 16)
            if general:
                for t in range(TT):
                    if t:
                        sp.wait_ge(s["bias_done"], t)
                    sp.dma_start(mask_i[:], d["mask"][0, 0, t * P:(t + 1) * P]).then_inc(s["mask_in"], 16)
                for t in range(NT):
                    sp.wait_ge(s["bias_done"], TT + t)
                    sp.dma_start(mask_i[0:rows(t), 0:S], d["maskT"][0, 0, t * P:t * P + rows(t)]).then_inc(s["mask_in"], 16)
            sp.wait_ge(s["init"], 5 * NB + (2 if general else 1))
            for j in range(NB):
                for h in range(HEADS):
                    sp.dma_start(Q[j][R_BIAS:R_BIAS + 1, h, :], orow[:]).then_inc(s["rows_in"], 16)
                    src = zrow if general else g["bias_row"]
                    sp.dma_start(K[j][R_BIAS:R_BIAS + 1, h, :], src[:, 0:NK]).then_inc(s["rows_in"], 16)

            def run(p, s_, t, e, uses):
                for stage, part, i, u in plan(p, s_, t, e, uses):
                    if (stage, part) == ("P", "ln"):
                        n, j, r = p
                        wait(sp, s["p_vps"], NC * (n - NB + 1), s["turns_s"])
                        sp.dma_start(ct[j][:], d["ctxT"][n, :, K0:KEYS]).then_inc(ct_in[j], 16)
                    if (stage, part) == ("P", "split"):
                        n, j, r = p
                        wait_alone(sp, s["p_parts"], n + 1, s["turns_s"])
                        if isinstance(n, int) and n == 0:
                            sp.wait_ge(s["rows_in"], 16 * NB * 2 * HEADS)
                        wait(sp, s["t_st"], HEADS * NC * (n - NB + 1), s["turns_s"])
                        for c, (qp, kp) in enumerate(PARTS):
                            sp.dma_start(Q[j][c * DK:(c + 1) * DK, :, :], parts[:, qp, 0:S]).then_inc(qk_in[j], 16)
                            sp.dma_start(K[j][c * DK:(c + 1) * DK, :, :], parts[:, kp, S:S + NK]).then_inc(qk_in[j], 16)
                    if (stage, part) == ("S", "row"):
                        n, j, r = s_
                        wait_alone(sp, s["s_ml"], 2 * n + i + 1, s["turns_s"])
                        for k in range(2):
                            sp.dma_start(Q[j][R_MAX + k:R_MAX + k + 1, i * HH:(i + 1) * HH, :], nmp[i][:, k, :]).then_inc(mx_in[j][i], 16)
            steps(sp, run)

        @block.gpsimd
        def _(pool):
            for j in range(NB):
                for f in (Q[j], K[j]):
                    nc.gpsimd.memset(f[32:64, :, :], 0.0).then_inc(s["init"], 1)
                    nc.gpsimd.memset(f[64:96, :, :], 0.0).then_inc(s["init"], 1)
                nc.gpsimd.memset(K[j][R_MAX:R_ALL, :, :], 1.0).then_inc(s["init"], 1)
            if general:
                nc.gpsimd.memset(zrow[:], 0.0).then_inc(s["init"], 1)
            nc.gpsimd.memset(orow[:], 1.0).then_inc(s["init"], 1)
            pool.wait_ge(s["init"], 5 * NB + (2 if general else 1))

            def run(p, s_, t, e, uses):
                for stage, part, i, u in plan(p, s_, t, e, uses):
                    if (stage, part) == ("P", "ln"):
                        n = p[0]
                        pool.wait_ge(s["p_mv"], n + 1)
                        nc.gpsimd.tensor_tensor(ve[:], mv[:, :, 1], g["eps"][:], ALU.add).then_inc(s["p_ve"], 1)
                        pool.wait_ge(s["p_ve"], n + 1)
                        nc.gpsimd.tensor_tensor(rs0[:], ve[:], g["mhalf"][:], ALU.pow).then_inc(s["p_pow"], 1)
                        pool.wait_ge(s["p_pow"], n + 1)
                        nc.gpsimd.tensor_tensor(rs[:], rs0[:], g["any_q"][:], ALU.mult).then_inc(s["p_rstd"], 1)
                    if (stage, part) == ("P", "split"):
                        n, j, r = p
                        pool.wait_ge(s["p_kc"], NC * (n + 1))
                        nc.gpsimd.tensor_tensor(rem[:], qk[:], parts[:, 0, :], ALU.subtract).then_inc(s["p_rem"], 1)
                        sent(pool, qk_in, p, 16 * 2 * len(PARTS))
                        wait_alone(pool, s["p_rem"], n + 1, s["turns_p"])
                        nc.gpsimd.tensor_copy(parts[:, 1, :], rem[:]).then_inc(s["p_mid"], 1)
                        pool.wait_ge(s["p_mid"], n + 1)
                        nc.gpsimd.tensor_tensor(parts[:, 2, :], rem[:], parts[:, 1, :], ALU.subtract).then_inc(s["p_parts"], 1)
                    if (stage, part) == ("S", "row"):
                        n = s_[0]
                        sent(pool, [x[i] for x in mx_in], s_, 32)
                        wait_alone(pool, s["misc_free"], u + 1, s["turns_p"])
                        nc.gpsimd.tensor_copy(nmp[i][:, 0, :], nmf[i][:]).then_inc(s["s_mh"], 1)
                        pool.wait_ge(s["s_mh"], 2 * n + i + 1)
                        nc.gpsimd.tensor_tensor(nmp[i][:, 1, :], nmf[i][:], nmp[i][:, 0, :], ALU.subtract).then_inc(s["s_ml"], 1)
            steps(pool, run)

        @block.tensor
        def _(pe):
            pe.wait_ge(s["w_in"], 64)
            pe.wait_ge(s["init_v"], NB)
            if general:
                pe.wait_ge(s["bias_done"], TT + NT)

            def run(p, s_, t, e, uses):
                for stage, part, i, u in plan(p, s_, t, e, uses):
                    if (stage, part) == ("P", "ln"):
                        n, j, r = p
                        pe.wait_ge(s["p_xn"], n + 1)
                        wait(pe, s["misc_free"], u)
                        for q in range(TT):
                            last = nc.tensor.transpose(misc[:, q * P:(q + 1) * P], xn[:, q, :], ident[:])
                        last.then_inc(s["misc_full"], 1)
                    elif (stage, part) == ("P", "q"):
                        n, j, r = p
                        wait(pe, s["misc_free"], u)
                        nc.tensor.matmul(misc[:, 0:S], WqT[:], xnT[:], start=True, stop=True).then_inc(s["misc_full"], 1)
                    elif (stage, part) == ("P", "kv"):
                        n, j, r = p
                        pe.wait_ge(ct_in[j], 16 * (r + 1))
                        wait(pe, s["s_red"], HEADS * TT * NC * (n if general else n - 1))
                        for c, (k0, w) in enumerate(CH):
                            wait(pe, s["p_kc"], NC * n + c)
                            nc.tensor.matmul(sbank[0][:, 0:w], WkT[:], ct[j][:, k0:k0 + w], start=True, stop=True).then_inc(s["p_kps"], 1)
                            wait(pe, s["p_vc"], NC * n + c)
                            for kt in range(k0 // P, -(-(k0 + w) // P)):
                                o = (kt * P - k0)
                                last = nc.tensor.matmul(sbank[1][0:rows(kt), o:o + P], ct[j][:, kt * P:kt * P + rows(kt)], WvT[:],
                                                        start=True, stop=True)
                            last.then_inc(s["p_vps"], 1)
                    elif (stage, part) == ("S", "max"):
                        n, j, r = s_
                        if i == 0:
                            pe.wait_ge(qk_in[j], 16 * 2 * len(PARTS) * (r + 1))
                            pe.wait_ge(s["p_kc"], NC * (n + 1) if (p is None or general) else NC * (p[0] + 1))
                            pe.wait_ge(s["p_vc"], NC * (n + 1) if (p is None or general) else NC * (p[0] + 1))
                        h, q = divmod(i, TT)
                        for c, (k0, w) in enumerate(CH):
                            x = i * NC + c
                            wait(pe, s["s_red"], HEADS * TT * NC * n + x - 1)
                            mm = nc.tensor.matmul(sbank[x % 2][:, 0:w], Q[j][0:R_MAX, h, q * P:(q + 1) * P], K[j][0:R_MAX, h, k0:k0 + w],
                                                  start=True, stop=not general)
                            if general:
                                mm = nc.tensor.matmul(sbank[x % 2][:, 0:w], g["identb"][:], bias_q[:, q, k0:k0 + w], start=False, stop=True)
                            mm.then_inc(s["s_ps"], 1)
                    elif (stage, part) == ("S", "row"):
                        n, j, r = s_
                        wait(pe, s["misc_free"], u)
                        pe.wait_ge(mx_done, HEADS * TT * n + (i + 1) * HH * TT)
                        for q in range(TT):
                            last = nc.tensor.transpose(misc[0:HH, q * P:(q + 1) * P], mx[:, q, i * HH:(i + 1) * HH], ident[:])
                        last.then_inc(s["misc_full"], 1)
                    elif (stage, part) == ("T", "head"):
                        n, j, r = t
                        gi, c, hh = i
                        h = gi * GRP + hh
                        x = (gi * NC + c) * GRP + hh
                        if c == 0 and hh == 0 and gi in (0, 2):
                            pe.wait_ge(mx_in[j][gi // 2], 32 * (r + 1))
                        wait(pe, s["t_exp"], HEADS * NC * n + x - 1)
                        k0, w = CH[c]
                        for kt in range(k0 // P, -(-(k0 + w) // P)):
                            o = (kt - k0 // P) * S
                            mm = nc.tensor.matmul(stb[x % 2][0:rows(kt), o:o + S], K[j][0:R_ALL, h, kt * P:kt * P + rows(kt)],
                                                  Q[j][0:R_ALL, h, :], start=True, stop=not general)
                            if general:
                                w_ = rows(kt)
                                mm = nc.tensor.matmul(stb[x % 2][0:w_, o:o + S], g["identb"][0:w_, 0:w_], bias_k[0:w_, kt, :],
                                                      start=False, stop=True)
                        mm.then_inc(s["t_st"], 1)
                    elif part == "pv":
                        n, j, r = t if stage == "T" else e
                        gi, c = i
                        pe.wait_ge(s["t_exp"], HEADS * NC * n + (gi * NC + c + 1) * GRP)
                        if c == 0:
                            wait(pe, s["t_ot"], 4 * n + gi)
                        k0, w = CH[c]
                        z = (gi * NC + c) % 2
                        for kt in range(k0 // P, -(-(k0 + w) // P)):
                            for hh in range(GRP):
                                o = (kt - k0 // P) * S
                                mm = nc.tensor.matmul(otb[hh * VW:(hh + 1) * VW, 0:S], V[j][0:rows(kt), kt, gi * GRP + hh, :],
                                                      pr[z][0:rows(kt), hh, o:o + S], start=(kt == 0), stop=(kt == NT - 1),
                                                      tile_position=(0, hh * VW))
                        mm.then_inc(s["t_pv"], 1)
                    elif part == "turn":
                        n = (t if stage == "T" else e)[0]
                        wait(pe, s["misc_free"], u)
                        pe.wait_ge(s["t_ot"], 4 * n + i + 1)
                        for q in range(TT):
                            last = nc.tensor.transpose(misc[:, q * P:(q + 1) * P], ots[:, q * P:(q + 1) * P], ident[:])
                        last.then_inc(s["misc_full"], 1)
                    elif part == "attT":
                        wait(pe, s["misc_free"], u)
                        for q in range(TT):
                            last = nc.tensor.transpose(misc[:, q * P:(q + 1) * P], att[:, q, :], ident[:])
                        last.then_inc(s["misc_full"], 1)
                    elif part == "wo":
                        wait(pe, s["misc_free"], u)
                        for q in range(TT):
                            last = nc.tensor.matmul(misc[:, q * P:(q + 1) * P], attT[:, q * P:(q + 1) * P], WoT[:], start=True, stop=True)
                        last.then_inc(s["misc_full"], 1)
            steps(pe, run)

        @block.scalar
        def _(act):
            def run(p, s_, t, e, uses):
                for stage, part, i, u in plan(p, s_, t, e, uses):
                    if (stage, part) == ("P", "ln"):
                        n = p[0]
                        act.wait_ge(s["misc_full"], u + 1)
                        nc.scalar.activation(xnT[:], misc[:, 0:S], ACT.Copy).then_inc(s["misc_free"], 1)
                    elif (stage, part) == ("P", "q"):
                        n = p[0]
                        act.wait_ge(s["misc_full"], u + 1)
                        wait(act, s["p_parts"], n)
                        sent(act, qk_in, p, 16 * 2 * len(PARTS))
                        nc.scalar.activation(qk[:, 0:S], misc[:, 0:S], ACT.Copy, scale=DK ** -0.5)
                        nc.scalar.activation(parts[:, 0, 0:S], misc[:, 0:S], ACT.Copy, scale=DK ** -0.5).then_inc(s["misc_free"], 1)
                    elif (stage, part) == ("P", "kv"):
                        n, j, r = p
                        for c, (k0, w) in enumerate(CH):
                            act.wait_ge(s["p_kps"], NC * n + c + 1)
                            nc.scalar.activation(qk[:, S + k0:S + k0 + w], sbank[0][:, 0:w], ACT.Copy)
                            nc.scalar.activation(parts[:, 0, S + k0:S + k0 + w], sbank[0][:, 0:w], ACT.Copy).then_inc(s["p_kc"], 1)
                            act.wait_ge(s["p_vps"], NC * n + c + 1)
                            wait(act, s["t_pv"], 4 * NC * (n - NB + 1))
                            full, t0 = w // P, k0 // P
                            if full:
                                last = nc.scalar.activation(V[j][:, t0:t0 + full, :, 0:DK], sbank[1][:, 0:full * P].rearrange("p (t h c) -> p t h c", h=HEADS, c=DK), ACT.Copy)
                            else:
                                last = nc.scalar.activation(V[j][0:w, t0, :, 0:DK], sbank[1][0:w, 0:P].rearrange("p (h c) -> p h c", c=DK), ACT.Copy)
                            last.then_inc(s["p_vc"], 1)
                    elif (stage, part) == ("S", "row"):
                        n, j, r = s_
                        act.wait_ge(s["misc_full"], u + 1)
                        wait(act, s["s_ml"], 2 * (n - 1) + i + 1)
                        nc.scalar.activation(nmf[i][:], misc[0:HH, 0:S], ACT.Copy, scale=-1.0).then_inc(s["misc_free"], 1)
                    elif (stage, part) == ("T", "head"):
                        n, j, r = t
                        gi, c, hh = i
                        x = (gi * NC + c) * GRP + hh
                        act.wait_ge(s["t_st"], HEADS * NC * n + x + 1)
                        if hh == 0:
                            wait(act, s["t_pv"], 4 * NC * n + gi * NC + c - 1)
                        k0, w = CH[c]
                        rw, cols = min(P, w), -(-w // P) * S
                        nc.scalar.activation(pr[(gi * NC + c) % 2][0:rw, hh, 0:cols], stb[x % 2][0:rw, 0:cols], ACT.Exp).then_inc(s["t_exp"], 1)
                    elif part == "out":
                        n = (t if stage == "T" else e)[0]
                        act.wait_ge(s["t_pv"], 4 * NC * n + (i + 1) * NC)
                        wait(act, s["t_rec"], 4 * n + i)
                        nc.scalar.activation(ots[:], otb[:, 0:S], ACT.Copy).then_inc(s["t_ot"], 1)
                    elif part == "attT":
                        act.wait_ge(s["misc_full"], u + 1)
                        nc.scalar.activation(attT[:], misc[:, 0:S], ACT.Copy).then_inc(s["misc_free"], 1)

            steps(act, run)

        @block.vector
        def _(dve):
            def run(p, s_, t, e, uses):
                for stage, part, i, u in plan(p, s_, t, e, uses):
                    if (stage, part) == ("P", "ln"):
                        n = p[0]
                        for q in range(TT):
                            last = nc.vector.bn_stats(st6[:, q, :], xs[:, n, q, :])
                        last.then_inc(s["p_ch"], 1)
                        wait_alone(dve, s["p_ch"], n + 1, s["turns"])
                        for q in range(TT):
                            last = nc.vector.bn_aggr(mv[:, q, :], st6[:, q, :])
                        last.then_inc(s["p_mv"], 1)
                        dve.wait_ge(s["p_rstd"], n + 1)
                        wait(dve, s["p_kc"], NC * n)
                        for q in range(TT):
                            last = nc.vector.tensor_scalar(xn[:, q, :], xs[:, n, q, :], mv[:, q, 0:1], rs[:, q:q + 1], ALU.subtract, ALU.mult)
                        last.then_inc(s["p_xn"], 1)
                    elif (stage, part) == ("S", "max"):
                        n, j, r = s_
                        h, q = divmod(i, TT)
                        if i % (HH * TT) == 0:
                            wait(dve, s["s_ml"], 2 * (n - 1) + i // (HH * TT) + 1)
                        for c, (k0, w) in enumerate(CH):
                            x = i * NC + c
                            dve.wait_ge(s["s_ps"], HEADS * TT * NC * n + x + 1)
                            o = mx[:, q, h:h + 1] if NC == 1 else mxc[:, q, h, c:c + 1]
                            nc.vector.tensor_reduce(o, sbank[x % 2][:, 0:w], AX.X, ALU.max).then_inc(s["s_red"], 1)
                        if NC > 1:
                            dve.wait_ge(s["s_red"], HEADS * TT * NC * n + (i + 1) * NC)
                            nc.vector.tensor_reduce(mx[:, q, h:h + 1], mxc[:, q, h, :], AX.X, ALU.max).then_inc(s["s_mx"], 1)
                    elif part == "turn":
                        n = (t if stage == "T" else e)[0]
                        dve.wait_ge(s["misc_full"], u + 1)
                        mv4 = misc[:, 0:S].rearrange("p (q h c) -> p q h c", q=TT, c=VW)
                        nc.vector.reciprocal(rec[:], mv4[:, :, :, DK]).then_inc(s["t_rec"], 1)
                        dve.wait_ge(s["t_rec"], 4 * n + i + 1)
                        a4 = att[:, :, i * 32:(i + 1) * 32].rearrange("p q (h c) -> p q h c", c=DK)
                        nc.vector.tensor_tensor(a4, mv4[:, :, :, 0:DK], rec[:].unsqueeze(3).broadcast_to([P, TT, GRP, DK]), ALU.mult).then_inc(s["misc_free"], 1)
                    elif part == "wo":
                        n = e[0]
                        dve.wait_ge(s["misc_full"], u + 1)
                        xv = xs[:, n, :, :].rearrange("p q c -> p (q c)")
                        nc.vector.scalar_tensor_tensor(out=xv, in0=misc[:, 0:S], scalar=tgate[:, 1:2], in1=xv,
                                                       op0=ALU.mult, op1=ALU.add).then_inc(s["misc_free"], 1)

            for j in range(NB):
                v3 = V[j][:].rearrange("p t h c -> p (t h) c")
                nc.vector.memset(v3[:, :, DK:DK + 1], 1.0)
                nc.vector.memset(v3[:, :, DK + 1:VW], 0.0).then_inc(s["init_v"], 1)
            if general:
                for q in range(TT):
                    dve.wait_ge(s["mask_in"], 16 * (q + 1))
                    nc.vector.tensor_scalar(bias_q[:, q, :], mask_i[:], 0.0, MASKED, ALU.is_equal, ALU.mult).then_inc(s["bias_done"], 1)
                for kt in range(NT):
                    dve.wait_ge(s["mask_in"], 16 * (TT + kt + 1))
                    nc.vector.tensor_scalar(bias_k[0:rows(kt), kt, :], mask_i[0:rows(kt), 0:S], 0.0, MASKED, ALU.is_equal, ALU.mult)\
                      .then_inc(s["bias_done"], 1)
            steps(dve, run)
            dve.wait_ge(s["misc_free"], 10 * B)


def build_quantized_ffn(nc, d, g, out):
    NCH = B * S // BANK
    TPC = BANK // P
    with ExitStack() as ctx:
        m = Mem(nc, ctx, g)
        sb = lambda n, sh, dt=F32: m.sb("q_" + n, sh, dt)
        ident, xs, tgate = g["ident"], g["xs"], g["tgate"]
        xt = xs[:].rearrange("p b t c -> p (b t) c")
        NTILE = B * TT
        raw = [sb(f"raw{i}", [P, FC, P]) for i in range(3)]
        bm, bs, bi = (sb(n, [P, 3, FC * P // BLK]) for n in ("bm", "bs", "bi"))
        wT = [sb(f"wT{i}", [P, FC, P]) for i in range(3)]
        st6, mv, ve, rs = sb("st6", [P, NTILE, 6]), sb("mv", [P, NTILE, 2]), sb("ve", [P, NTILE]), sb("rs", [P, NTILE])
        xn = [sb(f"xn{j}", [P, TPC, D]) for j in range(2)]
        xT = sb("xT", [P, NCH, BANK])
        G = sb("G", [P, NCH, FC, BANK])
        U = sb("U", [P, NCH, FC, BANK])
        T = [sb(f"T{j}", [P, FC, BANK]) for j in range(2)]
        pm = {n: sb("pm_" + n, [P, NCH]) for n in "xguho"}
        sc = {n: sb("sc_" + n, [P, 4]) for n in "xguho"}
        pre = {n: sb("pre_" + n, [P, 1]) for n in "guho"}
        half, ofac, rnd = sb("half", [P, 1]), sb("ofac", [P, 1]), sb("rnd", [P, 1])
        ob = [sb(f"ob{j}", [P, TPC, D]) for j in range(2)]
        bank = [m.ps(f"q_b{i}", BANK) for i in range(8)]
        s = {n: m.sem("q_" + n) for n in
             ("w_in w_b1 w_b2 w_bm w_ch w_q w_tps w_T st1 st ve rs xn xmx x_tps x_ev ax xq g_ps u_ps g_ev u_ev g_mx u_mx "
              "turns pr ar sc_ch sc rnd th ag qg au qu sg1 sg2 h hmx ah o omx ao oq mm y").split()}
        y_out = [m.sem(f"q_y_out{j}") for j in range(2)]
        block = ctx.enter_context(nc.Block())
        NAMES = "xguho"

        @block.sync
        def _(sp):
            sp.dma_start(raw[0][:], d["w_gate"].rearrange("(f p) c -> p f c", p=P)).then_inc(s["w_in"], 16)
            sp.dma_start(raw[1][:], d["w_up"].rearrange("(f p) c -> p f c", p=P)).then_inc(s["w_in"], 16)
            sp.dma_start(raw[2][:], d["w_down"].rearrange("p (f c) -> p f c", c=P)).then_inc(s["w_in"], 16)
            o = out.rearrange("b (t p) c -> p (b t) c", p=P)
            for j in range(2):
                sp.sem_inc(y_out[j], 16)
            with sp.Fori(0, NCH // 2) as i:
                for j in range(2):
                    wait_alone(sp, s["y"], i * 2 + j + 3, s["turns"])
                    sp.dma_start(o[:, bass.ds((i * 2 + j) * TPC, TPC), :], ob[j][:]).then_inc(y_out[j], 16)
            for j in range(2):
                sp.wait_ge(y_out[j], 16 * NCH // 2 + 16)

        @block.gpsimd
        def _(pool):
            pool.wait_ge(s["w_bm"], 1)
            ch = 0
            for i in range(3):
                blocks = raw[i][:].rearrange("p f (k b) -> p (f k) b", b=BLK)
                nc.gpsimd.tensor_tensor(blocks, blocks, bi[:, i, :].unsqueeze(2).broadcast_to([P, 12, BLK]), ALU.mult).then_inc(s["w_ch"], 1)
                pool.wait_ge(s["w_ch"], 3 * i + 1)
                nc.gpsimd.tensor_scalar(blocks, blocks, RND, None, ALU.add).then_inc(s["w_ch"], 1)
                pool.wait_ge(s["w_ch"], 3 * i + 2)
                nc.gpsimd.tensor_scalar(blocks, blocks, RND, None, ALU.subtract).then_inc(s["w_ch"], 1)
                pool.wait_ge(s["w_ch"], 3 * i + 3)
                nc.gpsimd.tensor_tensor(blocks, blocks, bs[:, i, :].unsqueeze(2).broadcast_to([P, 12, BLK]), ALU.mult).then_inc(s["w_q"], 1)
            pool.wait_ge(s["st"], NTILE)
            pool.wait_ge(s["w_q"], 3)
            nc.gpsimd.tensor_scalar(ve[:], mv[:, :, 1], EPS, None, ALU.add).then_inc(s["ve"], 1)
            pool.wait_ge(s["ve"], 1)
            nc.gpsimd.tensor_tensor(rs[:], ve[:], g["mhalf"][:, 0:1].broadcast_to([P, NTILE]), ALU.pow).then_inc(s["rs"], 1)
            for k, n in enumerate("xguho"):
                pool.wait_ge(s["pr"], k + 1)
                if k:
                    pool.wait_ge(s["ar"], k)
                nc.gpsimd.partition_all_reduce(sc[n][:, 1:2], sc[n][:, 0:1], P, bass.bass_isa.ReduceOp.max).then_inc(s["ar"], 1)

        @block.tensor
        def _(pe):
            for i in range(3):
                pe.wait_ge(s["w_q"], i + 1)
                for f in range(FC):
                    last = nc.tensor.transpose(bank[i][:, f * P:(f + 1) * P], raw[i][:, f, :], ident[:])
                last.then_inc(s["w_tps"], 1)
            with pe.Fori(0, NCH // 2) as i:
                for j in range(2):
                    n = i * 2 + j
                    pe.wait_ge(s["xn"], n + 1)
                    pe.wait_ge(s["x_ev"], n + 1)
                    for t in range(TPC):
                        last = nc.tensor.transpose(bank[3 + j][:, t * P:(t + 1) * P], xn[j][:, t, :], ident[:])
                    last.then_inc(s["x_tps"], 1)
            pe.wait_ge(s["w_T"], 3)
            with pe.Fori(0, NCH) as n:
                pe.wait_ge(s["xq"], n + 1)
                for f in range(FC):
                    pe.wait_ge(s["g_ev"], n * FC + f + 1)
                    nc.tensor.matmul(bank[f][:], wT[0][:, f, :], xT[:, n, :], start=True, stop=True).then_inc(s["g_ps"], 1)
                    pe.wait_ge(s["u_ev"], n * FC + f + 1)
                    nc.tensor.matmul(bank[5 + f][:], wT[1][:, f, :], xT[:, n, :], start=True, stop=True).then_inc(s["u_ps"], 1)
            with pe.Fori(0, NCH // 2) as i:
                for j in range(2):
                    n = i * 2 + j
                    pe.wait_ge(s["oq"], n + 1)
                    pe.wait_ge(s["y"], n + 1)
                    for t in range(TPC):
                        for f in range(FC):
                            last = nc.tensor.matmul(bank[3 + j][:, t * P:(t + 1) * P], T[j][:, f, t * P:(t + 1) * P], wT[2][:, f, :],
                                                    start=(f == 0), stop=(f == FC - 1))
                    last.then_inc(s["mm"], 1)

        @block.scalar
        def _(act):
            act.sem_inc(s["x_ev"], 2)
            act.sem_inc(s["g_ev"], FC)
            act.sem_inc(s["u_ev"], FC)
            for i in range(3):
                act.wait_ge(s["w_tps"], i + 1)
                nc.scalar.activation(wT[i][:].rearrange("p f c -> p (f c)"), bank[i][:, 0:FC * P], ACT.Copy).then_inc(s["w_T"], 1)
            with act.Fori(0, NCH // 2) as i:
                for j in range(2):
                    n = i * 2 + j
                    act.wait_ge(s["x_tps"], n + 1)
                    nc.scalar.activation(xT[:, n, :], bank[3 + j][:], ACT.Copy).then_inc(s["x_ev"], 1)
            act.wait_ge(s["rnd"], 1)

            def scaled(dst, src, tensor, done):
                nc.scalar.activation(dst, src, ACT.Identity, bias=rnd[:, 0:1], scale=sc[tensor][:, 3:4]).then_inc(s[done], 1)

            act.wait_ge(s["x_ev"], NCH + 2)
            act.wait_ge(s["sc"], 1)
            with act.Fori(0, NCH) as n:
                scaled(xT[:, n, :], xT[:, n, :], "x", "ax")
            with act.Fori(0, NCH) as n:
                for f in range(FC):
                    act.wait_ge(s["g_ps"], n * FC + f + 1)
                    nc.scalar.activation(G[:, n, f, :], bank[f][:], ACT.Copy).then_inc(s["g_ev"], 1)
                    act.wait_ge(s["u_ps"], n * FC + f + 1)
                    nc.scalar.activation(U[:, n, f, :], bank[5 + f][:], ACT.Copy).then_inc(s["u_ev"], 1)
            act.wait_ge(s["sc"], 2)
            with act.Fori(0, NCH) as n:
                scaled(G[:, n, :, :], G[:, n, :, :], "g", "ag")
            with act.Fori(0, NCH // 2) as i:
                for j in range(2):
                    n = i * 2 + j
                    act.wait_ge(s["qg"], n + 1)
                    act.wait_ge(s["h"], n + 1)
                    nc.scalar.activation(T[j][:], G[:, n, :, :], ACT.Tanh, scale=half[:, 0:1]).then_inc(s["th"], 1)
            act.wait_ge(s["sc"], 3)
            with act.Fori(0, NCH) as n:
                scaled(U[:, n, :, :], U[:, n, :, :], "u", "au")
            act.wait_ge(s["sc"], 4)
            with act.Fori(0, NCH) as n:
                scaled(G[:, n, :, :], G[:, n, :, :], "h", "ah")
            act.wait_ge(s["sc"], 5)
            with act.Fori(0, NCH // 2) as i:
                for j in range(2):
                    n = i * 2 + j
                    act.wait_ge(s["mm"], n + 1)
                    scaled(T[j][:], G[:, n, :, :], "o", "ao")

        @block.vector
        def _(dve):
            nc.vector.memset(rnd[:], RND).then_inc(s["rnd"], 1)
            dve.sem_inc(s["y"], 2)
            dve.sem_inc(s["h"], 2)
            dve.sem_inc(s["xmx"], 2)
            dve.wait_ge(s["w_in"], 48)
            for i in range(3):
                last = nc.vector.tensor_reduce(bm[:, i, :], raw[i][:].rearrange("p f (k b) -> p (f k) b", b=BLK), AX.X, ALU.max,
                                               apply_absolute_value=True)
            last.then_inc(s["w_b1"], 1)
            dve.wait_ge(s["w_b1"], 1)
            nc.vector.tensor_scalar(bs[:], bm[:], 1.0 / 7.0, 1e-12, ALU.mult, ALU.max).then_inc(s["w_b2"], 1)
            dve.wait_ge(s["w_b2"], 1)
            nc.vector.reciprocal(bi[:], bs[:]).then_inc(s["w_bm"], 1)
            with dve.Fori(0, NTILE // TPC) as n:
                for t in range(TPC):
                    nc.vector.bn_stats(st6[:, n * TPC + t, :], xt[:, n * TPC + t, :]).then_inc(s["st1"], 1)
            dve.wait_ge(s["st1"], NTILE)
            for t in range(NTILE):
                nc.vector.bn_aggr(mv[:, t, :], st6[:, t, :]).then_inc(s["st"], 1)
            dve.wait_ge(s["rs"], 1)
            with dve.Fori(0, NCH // 2) as i:
                for j in range(2):
                    n = i * 2 + j
                    dve.wait_ge(s["x_ev"], n + 1)
                    dve.wait_ge(s["xmx"], n + 1)
                    for t in range(TPC):
                        k = n * TPC + t
                        last = nc.vector.tensor_scalar(xn[j][:, t, :], xt[:, k, :], mv[:, k, 0:1], rs[:, bass.ds(k, 1)], ALU.subtract, ALU.mult)
                    last.then_inc(s["xn"], 1)
                    dve.wait_ge(s["xn"], n + 1)
                    nc.vector.tensor_reduce(pm["x"][:, bass.ds(n, 1)], xn[j][:], AX.XY, ALU.max, apply_absolute_value=True).then_inc(s["xmx"], 1)

            chain = Chain(dve, s["sc_ch"], 0, 0)

            def scale(k, n, before, count):
                dve.wait_ge(before, count)
                nc.vector.tensor_reduce(sc[n][:, 0:1], pm[n][:], AX.X, ALU.max).then_inc(s["pr"], 1)
                dve.wait_ge(s["ar"], k)
                m1 = sc[n][:, 1:2]
                if n == "x":
                    chain.mark(nc.vector.tensor_scalar(sc[n][:, 2:3], m1, 1.0 / QMAX, 1e-12, ALU.mult, ALU.max))
                    chain.sync()
                    nc.vector.reciprocal(sc[n][:, 3:4], sc[n][:, 2:3]).then_inc(s["sc"], 1)
                    dve.wait_ge(s["sc"], k)
                    return
                chain.mark(nc.vector.tensor_scalar(sc[n][:, 2:3], m1, pre[n][:, 0:1], 1.0 / QMAX, ALU.mult, ALU.mult))
                chain.sync()
                chain.mark(nc.vector.tensor_scalar(sc[n][:, 2:3], sc[n][:, 2:3], 1e-12, None, ALU.max))
                chain.sync()
                chain.mark(nc.vector.reciprocal(sc[n][:, 3:4], sc[n][:, 2:3]))
                chain.sync()
                if n == "g":
                    chain.mark(nc.vector.tensor_scalar(half[:], sc[n][:, 2:3], 0.5, None, ALU.mult))
                    chain.mark(nc.vector.tensor_scalar(pre["h"][:], sc[n][:, 2:3], 1.0 / 65536.0, None, ALU.mult))
                if n == "h":
                    chain.mark(nc.vector.tensor_tensor(pre["o"][:], sc["h"][:, 2:3], sc["u"][:, 2:3], ALU.mult))
                if n == "o":
                    chain.mark(nc.vector.tensor_tensor(ofac[:], sc["o"][:, 2:3], tgate[:, 3:4], ALU.mult))
                    chain.sync()
                nc.vector.tensor_tensor(sc[n][:, 3:4], sc[n][:, 3:4], pre[n][:], ALU.mult).then_inc(s["sc"], 1)
                dve.wait_ge(s["sc"], k)

            def round_off(x, done):
                nc.vector.tensor_scalar(x, x, RND, None, ALU.subtract).then_inc(s[done], 1)

            scale(1, "x", s["xmx"], NCH + 2)
            chain.mark(nc.vector.tensor_copy(pre["g"][:], sc["x"][:, 2:3]))
            chain.mark(nc.vector.tensor_copy(pre["u"][:], sc["x"][:, 2:3]))
            with dve.Fori(0, NCH) as n:
                dve.wait_ge(s["ax"], n + 1)
                round_off(xT[:, n, :], "xq")
            with dve.Fori(0, NCH) as n:
                dve.wait_ge(s["g_ev"], n * FC + 2 * FC)
                nc.vector.tensor_reduce(pm["g"][:, bass.ds(n, 1)], G[:, n, :, :], AX.XY, ALU.max, apply_absolute_value=True).then_inc(s["g_mx"], 1)
                dve.wait_ge(s["u_ev"], n * FC + 2 * FC)
                nc.vector.tensor_reduce(pm["u"][:, bass.ds(n, 1)], U[:, n, :, :], AX.XY, ALU.max, apply_absolute_value=True).then_inc(s["u_mx"], 1)
            scale(2, "g", s["g_mx"], NCH)
            scale(3, "u", s["u_mx"], NCH)
            with dve.Fori(0, NCH) as n:
                dve.wait_ge(s["ag"], n + 1)
                round_off(G[:, n, :, :], "qg")
            with dve.Fori(0, NCH // 2) as i:
                for j in range(2):
                    n = i * 2 + j
                    dve.wait_ge(s["th"], n + 1)
                    nc.vector.tensor_scalar(T[j][:], T[j][:], 32767.0 / 32768.0, 32768.0, ALU.min, ALU.mult).then_inc(s["sg1"], 1)
                    dve.wait_ge(s["sg1"], n + 1)
                    nc.vector.tensor_scalar(T[j][:], T[j][:], 32768.0 + RND, RND, ALU.add, ALU.subtract).then_inc(s["sg2"], 1)
                    dve.wait_ge(s["sg2"], n + 1)
                    nc.vector.tensor_tensor(G[:, n, :, :], T[j][:], G[:, n, :, :], ALU.mult).then_inc(s["h"], 1)
                    dve.wait_ge(s["h"], n + 3)
                    nc.vector.tensor_reduce(pm["h"][:, bass.ds(n, 1)], G[:, n, :, :], AX.XY, ALU.max, apply_absolute_value=True).then_inc(s["hmx"], 1)
            scale(4, "h", s["hmx"], NCH)
            with dve.Fori(0, NCH) as n:
                dve.wait_ge(s["au"], n + 1)
                round_off(U[:, n, :, :], "qu")
            dve.wait_ge(s["qu"], NCH)
            with dve.Fori(0, NCH) as n:
                dve.wait_ge(s["ah"], n + 1)
                nc.vector.scalar_tensor_tensor(out=G[:, n, :, :].rearrange("p f c -> p (f c)"), in0=G[:, n, :, :].rearrange("p f c -> p (f c)"),
                                               scalar=RND, in1=U[:, n, :, :].rearrange("p f c -> p (f c)"),
                                               op0=ALU.subtract, op1=ALU.mult).then_inc(s["o"], 1)
                dve.wait_ge(s["o"], n + 1)
                nc.vector.tensor_reduce(pm["o"][:, bass.ds(n, 1)], G[:, n, :, :], AX.XY, ALU.max, apply_absolute_value=True).then_inc(s["omx"], 1)
            scale(5, "o", s["omx"], NCH)
            dve.sem_inc(s["mm"], 2)

            def result(n, j):
                dve.wait_ge(s["mm"], n + 3)
                xv = xs[:].rearrange("p b t c -> p (b t c)")[:, bass.ds(n * BANK, BANK)]
                nc.vector.scalar_tensor_tensor(out=ob[j][:].rearrange("p t c -> p (t c)"), in0=bank[3 + j][:], scalar=ofac[:, 0:1], in1=xv,
                                               op0=ALU.mult, op1=ALU.add).then_inc(s["y"], 1)

            with dve.Fori(0, NCH // 2) as i:
                for j in range(2):
                    n = i * 2 + j
                    dve.wait_ge(s["ao"], n + 1)
                    round_off(T[j][:], "oq")
                    dve.wait_ge(y_out[j], i * 16 + 16)
                    result(n, j)


def build(nc, d, out, stop=9):
    with ExitStack() as ctx:
        m = Mem(nc, ctx)
        g = {
            "ctx": ctx, "sems": {},
            "ident": m.sb("ident", [P, P]), "identb": m.sb("identb", [P, P], BF16),
            "iota_i": m.sb("iota_i", [P, NEXP], I32), "iota": m.sb("iota", [P, NEXP]),
            "mhalf": m.sb("mhalf", [P, TT]), "eps": m.sb("eps", [P, TT]),
            "tgate": m.sb("tgate", [P, 4]), "any_q": m.sb("any_q", [P, TT]),
            "bias_row": m.sb("bias_row", [1, BANK], BF16), "tail_only": m.sb("tail_only", [1, 1], I32),
            "xs": m.sb("xs", [P, B, TT, D]),
        }
        build_setup(nc, d, g)
        build_attend_moe(nc, d, g)
        if stop == 1:
            dump(nc, g, out)
            return
        if stop == 4:
            build_quantized_ffn(nc, d, g, out)
            return
        tail_only = nc.values_load(g["tail_only"][0:1, 0:1], min_val=0, max_val=1)
        with nc.If(tail_only != 0):
            build_head_attention(nc, d, g, general=False)
        with nc.Else():
            build_head_attention(nc, d, g, general=True)
        if stop == 2:
            dump(nc, g, out)
            return
        build_quantized_ffn(nc, d, g, out)


def dump(nc, g, out):
    with ExitStack() as ctx:
        sem = ctx.enter_context(nc.semaphore("dumped"))
        block = ctx.enter_context(nc.Block())

        @block.sync
        def _(sp):
            sp.dma_start(out.rearrange("b (t p) c -> p b t c", p=P), g["xs"][:]).then_inc(sem, 16)
            sp.wait_ge(sem, 16)


def layouts(i):
    T = lambda a: np.ascontiguousarray(np.swapaxes(np.asarray(a), -1, -2))
    N = lambda a: np.ascontiguousarray(np.asarray(a))
    dk_major = lambda a: np.ascontiguousarray(a.reshape(P, HEADS, DK).transpose(0, 2, 1).reshape(P, P))
    return {
        "x": N(i["x"]), "ctx": N(i["ctx_1024"]), "ctxT": T(i["ctx_1024"]),
        "mask": N(i["mask_1x1xSxS2_ik0"]), "maskT": T(i["mask_1x1xSxS2_ik0"]),
        "g_xattn": N(i["g_xattn"]), "g_ffn": N(i["g_ffn"]),
        "L0_WT": T(i["L0_xattn_W"]), "L0_xattn_b": N(i["L0_xattn_b"]),
        "router_wT": T(i["L0_ffn_router_w"]), "gate_up_w": N(i["L0_ffn_gate_up_w"]), "down_w": N(i["L0_ffn_down_w"]),
        "shared_gateT": T(i["L0_ffn_shared_gate_w"]), "shared_upT": T(i["L0_ffn_shared_up_w"]),
        "shared_downT": T(i["L0_ffn_shared_down_w"]),
        "WqT": dk_major(T(i["L1_xattn_Wq"])), "WkT": dk_major(T(i["L1_xattn_Wk"])), "WvT": T(i["L1_xattn_Wv"]), "WoT": T(i["L1_xattn_Wo"]),
        "w_gate": N(i["L1_ffn_w_gate"]), "w_up": N(i["L1_ffn_w_up"]), "w_down": N(i["L1_ffn_w_down"]),
    }


def kernel(**inputs):
    import concourse.bacc as bacc
    from concourse.bass_utils import run_bass_kernel_spmd

    nc = bacc.Bacc("TRN2", target_bir_lowering=False, num_devices=1)
    arrays = layouts(inputs)
    d = {k: nc.dram_tensor(f"in_{k}", a.shape, mybir.dt.from_np(a.dtype), kind="ExternalInput").ap() for k, a in arrays.items()}
    out = nc.dram_tensor("out_x", (B, S, D), F32, kind="ExternalOutput").ap()
    build(nc, d, out)
    r = run_bass_kernel_spmd(nc, [{f"in_{k}": a for k, a in arrays.items()}], core_ids=[0])
    return r.results[0]["out_x"]
```
